# Optimizing a Trainium2 kernel written in Bass

```python
import numpy as np
import jax
import jax.numpy as jnp

def _softmax(x, axis=-1):
    return jax.nn.softmax(x, axis=axis)

def _gelu(x):
    return jax.nn.gelu(x, approximate=True)

def _silu(x):
    return jax.nn.silu(x)

def _sigmoid(x):
    return jax.nn.sigmoid(x)

def _layernorm(x, axis=-1, eps=1e-05):
    m = jnp.mean(x, axis=axis, keepdims=True)
    v = jnp.var(x, axis=axis, keepdims=True)
    return (x - m) / jnp.sqrt(v + eps)

def _scatter_add(tgt, idx, src, axis=0):
    return tgt.at[idx].add(src)

def _segment_sum(src, seg, n):
    return jax.ops.segment_sum(src, seg, n)
kernel_name = 'mk_adaln_d1_jaxref_r8_2c10f5'

def setup_inputs(seed: int=0):
    np.random.seed(seed)
    _w = jnp.asarray

    def _L0_attn_setup():
        import jax, jax.numpy as jnp
        import numpy as np
        import math
        FEATURE_DIM = 16
        NUM_HEADS = 16
        HIDDEN = 128
        HEAD_DIM = HIDDEN // NUM_HEADS
        EPS = 1e-12
        IU, JU = np.triu_indices(FEATURE_DIM, 1)
        RD = math.sqrt(FEATURE_DIM)
        RRD = math.sqrt(RD)
        R2 = math.sqrt(2.0)

        def taylor_feature_map(x):
            x2 = x[..., :, None] * x[..., None, :]
            off = x2[..., IU, JU]
            diag = jnp.square(x)
            ones = jnp.ones_like(x[..., :1])
            return jnp.concatenate([ones, x / RRD, diag / (RD * R2), off / RD], axis=-1)
        key = jax.random.key(seed)
        k0, k1, k2, k3, k4 = jax.random.split(key, 5)
        b, t = (2, 64)
        s = 1.0 / math.sqrt(HIDDEN)
        return {'hidden_states': jax.random.normal(k0, (b, t, HIDDEN), jnp.float32), 'Wq': jax.random.normal(k1, (NUM_HEADS * FEATURE_DIM, HIDDEN), jnp.float32) * s, 'Wk': jax.random.normal(k2, (NUM_HEADS * FEATURE_DIM, HIDDEN), jnp.float32) * s, 'Wv': jax.random.normal(k3, (HIDDEN, HIDDEN), jnp.float32) * s, 'Wo': jax.random.normal(k4, (HIDDEN, HIDDEN), jnp.float32) * s}
    _L0_attn_in = _L0_attn_setup()

    def _L0_ffn_setup():
        import jax, jax.numpy as jnp
        import numpy as np
        CAPACITY_FACTOR = 1.0
        key = jax.random.key(seed)
        ks = jax.random.split(key, 5)
        B, S, D, E, F = (2, 256, 128, 8, 512)
        x = jax.random.normal(ks[0], (B, S, D), dtype=jnp.float32)
        Ws = jax.random.normal(ks[1], (D, E), dtype=jnp.float32) * (1.0 / np.sqrt(D))
        bs = jnp.zeros((E,), dtype=jnp.float32)
        W1 = jax.random.normal(ks[2], (E, D, F), dtype=jnp.float32) * (1.0 / np.sqrt(D))
        b1 = jnp.zeros((E, F), dtype=jnp.float32)
        W2 = jax.random.normal(ks[3], (E, F, D), dtype=jnp.float32) * (1.0 / np.sqrt(F))
        b2 = jnp.zeros((E, D), dtype=jnp.float32)
        return {'x': x, 'Ws': Ws, 'bs': bs, 'W1': W1, 'b1': b1, 'W2': W2, 'b2': b2}
    _L0_ffn_in = _L0_ffn_setup()
    _L0_c = _w((lambda *s: np.random.randn(*s).astype(np.float32) * 0.05)(16, 128))
    _L0_wmod = _w((lambda *s: np.random.randn(*s).astype(np.float32) * 0.05)(128, 6 * 128) * 128 ** (-0.5))
    _d = {'L0_attn_hidden_states': _L0_attn_in['hidden_states'], 'L0_attn_Wq': _L0_attn_in['Wq'], 'L0_attn_Wk': _L0_attn_in['Wk'], 'L0_attn_Wv': _L0_attn_in['Wv'], 'L0_attn_Wo': _L0_attn_in['Wo'], 'L0_ffn_Ws': _L0_ffn_in['Ws'], 'L0_ffn_bs': _L0_ffn_in['bs'], 'L0_ffn_W1': _L0_ffn_in['W1'], 'L0_ffn_b1': _L0_ffn_in['b1'], 'L0_ffn_W2': _L0_ffn_in['W2'], 'L0_ffn_b2': _L0_ffn_in['b2'], 'L0_c': _L0_c, 'L0_wmod': _L0_wmod}
    _x0 = _d['L0_attn_hidden_states']
    _d['L0_attn_hidden_states'] = jax.random.normal(jax.random.fold_in(jax.random.key(seed), 1), (16, 256, 128), dtype=_x0.dtype)
    del _x0
    return _d

def reference(L0_attn_hidden_states, L0_attn_Wq, L0_attn_Wk, L0_attn_Wv, L0_attn_Wo, L0_ffn_Ws, L0_ffn_bs, L0_ffn_W1, L0_ffn_b1, L0_ffn_W2, L0_ffn_b2, L0_c, L0_wmod):

    def _L0_attn_ref(hidden_states, Wq, Wk, Wv, Wo):
        import jax, jax.numpy as jnp
        import numpy as np
        import math
        FEATURE_DIM = 16
        NUM_HEADS = 16
        HIDDEN = 128
        HEAD_DIM = HIDDEN // NUM_HEADS
        EPS = 1e-12
        IU, JU = np.triu_indices(FEATURE_DIM, 1)
        RD = math.sqrt(FEATURE_DIM)
        RRD = math.sqrt(RD)
        R2 = math.sqrt(2.0)

        def taylor_feature_map(x):
            x2 = x[..., :, None] * x[..., None, :]
            off = x2[..., IU, JU]
            diag = jnp.square(x)
            ones = jnp.ones_like(x[..., :1])
            return jnp.concatenate([ones, x / RRD, diag / (RD * R2), off / RD], axis=-1)
        b, t, _ = hidden_states.shape
        q = (hidden_states @ Wq.T).reshape(b, t, NUM_HEADS, FEATURE_DIM).transpose(0, 2, 1, 3)
        k = (hidden_states @ Wk.T).reshape(b, t, NUM_HEADS, FEATURE_DIM).transpose(0, 2, 1, 3)
        v = (hidden_states @ Wv.T).reshape(b, t, NUM_HEADS, HEAD_DIM).transpose(0, 2, 1, 3)
        q = taylor_feature_map(q)
        k = taylor_feature_map(k)
        kv = jnp.cumsum(k[..., None, :] * v[..., :, None], axis=2)
        y = jnp.einsum('bhtD,bhtdD->bhtd', q, kv)
        z = jnp.cumsum(k, axis=2)
        denom = jnp.sum(q * z, axis=-1, keepdims=True) + EPS
        y = y / denom
        y = y.transpose(0, 2, 1, 3).reshape(b, t, NUM_HEADS * HEAD_DIM)
        return y @ Wo.T

    def _L0_ffn_ref(x, Ws, bs, W1, b1, W2, b2):
        import jax, jax.numpy as jnp
        import numpy as np
        CAPACITY_FACTOR = 1.0
        B, S, D = x.shape
        E = Ws.shape[1]
        N = B * S
        k = int(CAPACITY_FACTOR * N / E)
        xf = x.reshape(N, D)
        route_prob = jax.nn.softmax(xf @ Ws + bs, axis=-1).T
        route_vals, routes = jax.lax.top_k(route_prob, k)
        xin = xf[routes]
        h = jax.nn.gelu(jnp.einsum('ekd,edf->ekf', xin, W1) + b1[:, None, :])
        out = jnp.einsum('ekf,efd->ekd', h, W2) + b2[:, None, :]
        out = out * route_vals[..., None]
        final = jnp.zeros((N, D), dtype=x.dtype).at[routes.reshape(-1)].add(out.reshape(-1, D))
        return final.reshape(B, S, D)
    x = L0_attn_hidden_states
    mod = (_silu(L0_c) @ L0_wmod).reshape(L0_c.shape[0], 6, 1, -1)
    sa, ca, ga, sb, cb, gb = (mod[:, 0], mod[:, 1], mod[:, 2], mod[:, 3], mod[:, 4], mod[:, 5])
    ga = (2 * (ga >= 0) - 1) * jnp.maximum(jnp.abs(ga), 0.25)
    gb = (2 * (gb >= 0) - 1) * jnp.maximum(jnp.abs(gb), 0.25)
    h = _layernorm(x, axis=-1) * (1 + ca) + sa
    x = x + ga * _L0_attn_ref(h, L0_attn_Wq, L0_attn_Wk, L0_attn_Wv, L0_attn_Wo)
    h = _layernorm(x, axis=-1) * (1 + cb) + sb
    x = x + gb * _L0_ffn_ref(h, L0_ffn_Ws, L0_ffn_bs, L0_ffn_W1, L0_ffn_b1, L0_ffn_W2, L0_ffn_b2)
    return x

_drawn_inputs = setup_inputs


def setup_inputs(seed=0):
    import zlib

    import numpy as np

    out = dict(_drawn_inputs(seed))
    spreads = {'L0_ffn_bs': (0.0, 0.8), 'L0_ffn_b1': (0.0, 0.8), 'L0_ffn_b2': (0.0, 0.8)}
    factors = {}
    for name, (base, spread) in spreads.items():
        noise = np.random.default_rng([zlib.crc32(name.encode()), seed]).standard_normal(out[name].shape)
        drawn = base * np.exp(spread * noise) if base else spread * noise
        out[name] = jnp.asarray(drawn.astype(out[name].dtype))
    for name, factor in factors.items():
        out[name] = (out[name] * factor).astype(out[name].dtype)
    return out
```

```python
import concourse.bass as bass
from concourse import mybir
from contextlib import ExitStack


def adaln_block_kernel(
    nc: bass.Bass,
    x: bass.AP,
    wqk: bass.AP,
    wv: bass.AP,
    wo: bass.AP,
    ws: bass.AP,
    bs: bass.AP,
    w1: bass.AP,
    b1: bass.AP,
    w2: bass.AP,
    b2: bass.AP,
    c: bass.AP,
    wmod: bass.AP,
    out: bass.AP,
):
    fp32 = mybir.dt.float32
    bf16 = mybir.dt.bfloat16
    i32 = mybir.dt.int32
    u32 = mybir.dt.uint32
    ALU = mybir.AluOpType
    ACT = mybir.ActivationFunctionType
    AX = mybir.AxisListType

    P = 128
    NTOK, D = x.shape
    NB = c.shape[0]
    SEQ = NTOK // NB
    NT = NTOK // P
    HD = 8
    PAIRS = D // HD // 2
    FD = 16
    SECT = 6
    UT = 4
    UTOK = UT * P
    UNITS = NT // UT
    BK = 64
    NE = ws.shape[1]
    F = w1.shape[2]
    FC = F // P
    CAP = NTOK // NE
    CT = CAP // P
    EPS_LN = 1e-5
    EPS_DEN = 2e-12
    ROW = 2 * D + NE
    QPART = [0, 0, 0, 1, 1, 2]
    KPART = [0, 1, 2, 0, 1, 0]
    PARTS = [QPART, KPART, QPART, KPART]
    COL3, COL0, COL1 = 0, 64, 320

    rows = nc.dram_tensor("token_rows", (NTOK, ROW), fp32).ap()
    modrow = nc.dram_tensor("mod_rows", (3, NB * D), fp32).ap()

    ctx = ExitStack()
    with ctx:
        def sb(name, shape, dt):
            return ctx.enter_context(nc.sbuf_tensor(name, shape, dt))

        def sem(name):
            return ctx.enter_context(nc.semaphore(name))

        xall = sb("xall", [P, NT, D], fp32)
        b1_sb = sb("b1_sb", [P, NE, FC], fp32)
        b2_sb = sb("b2_sb", [P, NE, D], fp32)
        bs_sb = sb("bs_sb", [P, NE], fp32)
        ws_sb = sb("ws_sb", [P, NE], fp32)
        wqk_sb = sb("wqk_sb", [P, 4, P], fp32)
        wv_sb = sb("wv_sb", [P, 2, PAIRS * HD], fp32)
        wo_sb = sb("wo_sb", [P, D], fp32)
        ident = sb("ident", [P, P], fp32)
        ones_f = sb("ones_f", [P, P], fp32)
        mask = sb("mask", [P, 2, BK], fp32)
        half_neg = sb("half_neg", [P, NT], fp32)
        modb = sb("modb", [P, 3, NB, D], fp32)
        ga_sb, cb_sb, sb_sb = (modb[:, n, :, :] for n in range(3))
        ca_t = sb("ca_t", [P, NB], fp32)
        sa_t = sb("sa_t", [P, NB], fp32)
        c_t = sb("c_t", [P, NB], fp32)
        stats1 = sb("stats1", [P, NT, 6], fp32)
        mom1 = sb("mom1", [P, NT, 2], fp32)
        vare1 = sb("vare1", [P, NT], fp32)
        rstd1 = sb("rstd1", [P, NT], fp32)
        xn1 = sb("xn1", [P, UT, D], fp32)
        h_t = sb("h_t", [P, UTOK], fp32)
        part = [[sb(f"part{b}{n}", [P, UTOK], bf16) for n in range(3)] for b in range(2)]
        resid = [sb(f"resid{b}", [P, UTOK], fp32) for b in range(2)]
        area = sb("area", [P, 4, 16, UTOK], bf16)
        qs = [area[0:SECT * FD, 2 * p, :, :] for p in range(2)]
        ks = [area[0:SECT * FD, 2 * p + 1, :, :] for p in range(2)]
        area_f = area[:, :, :, :].rearrange("p a h t -> p (a h t)").bitcast(fp32)
        HALF = 2 * 16 * UTOK // 2
        wmod_sb = area_f[:, HALF:HALF + 6 * D]
        taken = [HALF + 6 * D]

        def small(n):
            at = taken[0]
            taken[0] += n * D
            v = area_f[0:NB, at:at + n * D]
            return v if n == 1 else v.rearrange("b (n d) -> b n d", n=n)

        c_sb, c_exp, c_den, c_sig, c_silu = (small(1) for _ in range(5))
        mod_sb, g_sign, g_mag, modout = small(6), small(2), small(2), small(4)
        iota_i = area_f[:, taken[0]:taken[0] + 32 * NT].bitcast(i32)
        area_b = area[:, :, :, :].rearrange("p a h t -> p (a h t)")
        oh_lo = area_b[:, 0:NE * 32 * NT].rearrange("p (e v t) -> p e v t", e=NE, v=32)
        at = NE * 32 * NT
        oh_hi = area_b[:, at:2 * at].rearrange("p (e a v t) -> p e a v t", e=NE, a=2, v=16)
        xg = [area_f[:, HALF + n * CT * ROW:HALF + (n + 1) * CT * ROW].rearrange("p (j r) -> p j r", j=CT)
              for n in range(4)]
        at = HALF + 4 * CT * ROW
        g_sb = area_f[:, at:at + FC * CAP].rearrange("p (k s) -> p k s", k=FC)
        at += FC * CAP
        x_t = [area_f[:, at + n * CAP:at + (n + 1) * CAP] for n in range(2)]
        at += 2 * CAP
        o_b = area_f[:, at:at + CT * D].rearrange("p (j d) -> p j d", j=CT)
        w1_sb = xall[:, :, :].rearrange("p t d -> p (t d)").rearrange("p (e f) -> p e f", e=NE)
        w2_sb = modb[:, 0:2, :, :].rearrange("p a b d -> p (a b d)").rearrange("p (e k d) -> p e k d", e=NE, k=FC)
        v_bd = [sb(f"v_bd{p}", [P, UTOK // BK, PAIRS, 32], fp32) for p in range(2)]
        wgt = [sb(f"wgt{p}", [P, 4, 512], fp32) for p in range(2)]
        wgt2 = [sb(f"wgt2{p}", [P, 4, 128], fp32) for p in range(2)]
        csum = sb("csum", [P, 4], fp32)
        y_t = sb("y_t", [P, 2, 2, SEQ], fp32)
        den = sb("den", [P, 16, 2], fp32)
        rec = sb("rec", [P, 16, 2], fp32)
        y_tok = sb("y_tok", [P, 2, D], fp32)
        y_d = sb("y_d", [P, SEQ], fp32)
        gated = sb("gated", [P, 2, D], fp32)
        x1 = [sb(f"x1_{b}", [P, 2, D], fp32) for b in range(2)]
        stats2 = sb("stats2", [P, 2, 6], fp32)
        mom2 = sb("mom2", [P, 2, 2], fp32)
        vare2 = sb("vare2", [P, 2], fp32)
        rstd2 = sb("rstd2", [P, 2], fp32)
        xn2 = sb("xn2", [P, 2, D], fp32)
        h2c = sb("h2c", [P, 2, D], fp32)
        h2 = [sb(f"h2_{b}", [P, 2, D], fp32) for b in range(2)]
        h2_t = sb("h2_t", [P, SEQ], fp32)
        lg = sb("lg", [P, NE, NT], fp32)

        mx = sb("mx", [P, NT], fp32)
        sh = sb("sh", [P, NE, NT], fp32)
        ex = sb("ex", [P, NE, NT], fp32)
        sm = sb("sm", [P, NT], fp32)
        rsm = sb("rsm", [P, NT], fp32)
        pr = sb("pr", [P, NE, NT], fp32)
        pr_te = sb("pr_te", [P, NT, NE], fp32)
        p_t = sb("p_t", [P, 2, P], fp32)
        hit = sb("hit", [P, 6, P], bf16)
        cnt = sb("cnt", [P, 6], fp32)
        blk = sb("blk", [P, P], fp32)
        cand = sb("cand", [P, 2], fp32)
        cand_low = sb("cand_low", [P, 2], fp32)
        cand3 = sb("cand3", [P, 2, 3], fp32)
        next3 = sb("next3", [P, 2, 3], fp32)
        steps = sb("steps", [P, 2, 4], fp32)
        next_steps = sb("next_steps", [P, 2, 4], fp32)
        reached = sb("reached", [P, 2, 3], fp32)
        steps_up = sb("steps_up", [P, 2], fp32)
        upd = sb("upd", [P, 2], fp32)
        thr_d = sb("thr_d", [P, 2, 4], fp32)
        thr = sb("thr", [P, NE], fp32)
        upper = sb("upper", [P, P], bf16)
        ones_b = sb("ones_b", [P, P], bf16)
        not_first = sb("not_first", [P, 2 * NE, NT], bf16)
        iota_v = sb("iota_v", [P, 32, NT], bf16)
        iota_t = sb("iota_t", [P, 16, NT], bf16)
        iota_p = sb("iota_p", [P, 1], fp32)
        pick = sb("pick", [P, 2, NE, NT], bf16)
        seen = sb("seen", [P, 2, NE, NT], bf16)
        seen_x = sb("seen_x", [P, 2, NE, NT], bf16)
        cgt = sb("cgt", [P, NE], fp32)
        pos = sb("pos", [P, 2, NE, NT], fp32)
        pos_m = sb("pos_m", [P, NE, NT], fp32)
        pos_i = sb("pos_i", [P, NE, NT], i32)
        lo_i = sb("lo_i", [P, NE, NT], i32)
        hi_i = sb("hi_i", [P, NE, NT], i32)
        lo_b = sb("lo_b", [P, NE, NT], bf16)
        hi_b = sb("hi_b", [P, NE, NT], bf16)
        idx_p = sb("idx_p", [P, NE, 16], fp32)
        idx_s = sb("idx_s", [P, NE, 16], i32)
        idx = sb("idx", [P, NE, CT], i32)
        o_sb = [sb(f"o_sb{n}", [P, CT, D], fp32) for n in range(2)]

        ps = ctx.enter_context(nc.psum_tensor("ps", [P, 8, 512], fp32))
        B_S2, B_PV, B_FR, B_PO = 4, 5, 6, 7

        s_x = sem("x_loaded")
        s_wa = sem("attention_weights_loaded")
        s_wf = sem("ffn_weights_loaded")
        s_c = sem("cond_loaded")
        s_k0 = sem("consts_zeroed")
        s_const = sem("consts_ready")
        s_vz = sem("v_zeroed")
        s_vinit = sem("v_ones_ready")
        s_mod = [sem(f"mod_step{n}") for n in range(12)]
        s_modst = sem("mod_rows_stored")
        s_bc = sem("mod_broadcast")
        s_gbrow = sem("gb_rows_stored")

        s_st1 = sem("ln1_stats")
        s_mo1 = sem("ln1_moments")
        s_ve1 = sem("ln1_var_eps")
        s_rs1 = sem("ln1_rstd")
        s_xn1 = sem("xn1_ready")
        s_htp = sem("h_t_psum")
        s_ht = sem("h_t_ready")
        s_qkp = sem("qk_psum")
        s_p1 = sem("part_high")
        s_re = sem("residual_ready")
        s_p2 = sem("part_middle")
        s_p3 = sem("part_low")
        s_stk = [sem(f"stack_dma{b}") for b in range(2)]
        s_vp = sem("v_psum")
        s_va = sem("v_even_ready")
        s_vb = sem("v_odd_ready")

        s_scA = sem("score_banks")
        s_scB = sem("score_bank2")
        s_sqA = sem("squared_banks")
        s_sqB = sem("squared_bank2")
        s_mk = sem("masked")
        s_pv = sem("pv_done")
        s_cs = sem("csum_ready")
        s_yt = sem("y_t_ready")

        s_ya = sem("y_token_psum")
        s_den = sem("den_ready")
        s_rec = sem("rec_ready")
        s_yn = sem("y_normalised")
        s_ydp = sem("y_d_psum")
        s_yd = sem("y_d_ready")
        s_at = sem("attn_psum")
        s_ga = sem("gated_ready")
        s_x1 = sem("x1_ready")
        s_x1o = [sem(f"x1_stored{b}") for b in range(2)]
        s_st2 = sem("ln2_stats")
        s_mo2 = sem("ln2_moments")
        s_ve2 = sem("ln2_var_eps")
        s_rs2 = sem("ln2_rstd")
        s_xn2 = sem("xn2_ready")
        s_h2c = sem("h2_scaled")
        s_h2 = sem("h2_ready")
        s_h2o = [sem(f"h2_stored{b}") for b in range(2)]
        s_h2p = sem("h2_t_psum")
        s_h2t = sem("h2_t_ready")
        s_lgp = sem("logits_psum")
        s_lg = sem("logits_ready")

        s_cb = sem("routing_consts_ready")
        s_ci = sem("iota_ready")
        s_bias = sem("ffn_biases_loaded")
        s_blk = sem("quadrant_blocks_ready")
        s_r = sem("routing_vector_step")
        s_sh = sem("logits_shifted")
        s_ex = sem("exp_ready")
        s_pr = sem("probs_ready")
        s_pte = sem("probs_by_token")
        s_pro = sem("probs_stored")
        s_ptp = sem("probs_t_psum")
        s_cmp = sem("compared")
        s_cnt = sem("counted")
        s_nxt = sem("next_candidates_ready")
        s_low = sem("cand_low_ready")
        s_upd = sem("update_ready")
        s_cand = sem("cand_ready")
        s_td = sem("threshold_spread")
        s_thp = sem("threshold_psum")
        s_seen = sem("seen_ready")
        s_posp = sem("positions_psum")
        s_ohh = sem("high_one_hot_ready")
        s_ohp = sem("high_one_hot_times_partition")
        s_oh = sem("one_hots_ready")
        s_ixp = sem("index_psum")
        s_ixc = sem("index_copied")
        s_idx = sem("index_ready")
        s_xg = [sem(f"gathered{n}") for n in range(4)]
        s_xtp = sem("x_t_psum")
        s_xt = sem("x_t_ready")
        s_h1 = sem("hidden_psum")
        s_g = sem("gelu_ready")
        s_op = sem("expert_psum")
        s_ob = sem("expert_biased")
        s_o = sem("expert_ready")
        s_sc = sem("scattered")
        EXP_STEPS = [32, 16, 8, 4, 2, 1]
        QUARTERINGS = 12

        NX = 4

        def wait(eng, s, v):
            if isinstance(v, int) and v <= 0:
                return
            eng.wait_ge(s, v)

        def units(eng, unit):
            unit(0, 0, True, False)
            with eng.Fori(0, (UNITS - 2) // 2) as it:
                for par in (1, 0):
                    unit(it * 2 + (2 - par), par, False, False)
            unit(UNITS - 1, 1, False, True)

        s_turn = sem("turn")

        def alone(eng):
            eng.sem_inc(s_turn, 1)

        block = ctx.enter_context(nc.Block())

        @block.sync
        def _(eng):
            eng.dma_start(c_sb[:, :], c).then_inc(s_c, 16)
            for bb in range(2):
                eng.sem_inc(s_x1o[bb], 16)
                eng.sem_inc(s_h2o[bb], 16)
            xv = x.rearrange("(t p) d -> p t d", p=P)
            eng.dma_start(xall[:, 0:UT, :], xv[:, 0:UT, :]).then_inc(s_x, 16)
            eng.dma_start(wmod_sb, wmod).then_inc(s_mod[10], 16)
            eng.dma_start(wqk_sb[:, :, :], wqk.rearrange("p (g m) -> p g m", g=4)).then_inc(s_wa, 16)
            eng.dma_start(wv_sb[:, :, :], wv.rearrange("p (a m) -> p a m", a=2)).then_inc(s_wa, 16)
            eng.dma_start(wo_sb[:, :], wo).then_inc(s_wa, 16)
            eng.dma_start(ws_sb[:, :], ws).then_inc(s_wa, 16)
            eng.dma_start(bs_sb[:, :], bs.unsqueeze(0).broadcast_to([P, NE])).then_inc(s_wa, 16)
            eng.wait_ge(s_x, 16)
            for n in range(1, NX):
                t0 = UT + (n - 1) * (NT - UT) // (NX - 1)
                t1 = UT + n * (NT - UT) // (NX - 1)
                eng.dma_start(xall[:, t0:t1, :], xv[:, t0:t1, :]).then_inc(s_x, 16)
            eng.wait_ge(s_mod[9], 1)
            for n in range(3):
                eng.dma_start(modrow[n, :].rearrange("(b d) -> b d", b=NB), modout[:, n, :])\
                   .then_inc(s_modst, 16)
            eng.wait_ge(s_modst, 48)
            for n, t in enumerate((ga_sb, cb_sb, sb_sb)):
                eng.dma_start(t[:, :, :].rearrange("p b d -> p (b d)"),
                              modrow[n, :].unsqueeze(0).broadcast_to([P, NB * D])).then_inc(s_bc, 16)
            def stacks(n, par, gi):
                eng.wait_ge(s_p3, n + 1)
                dst = (qs, ks)[gi % 2][par]
                g = gi // 2
                for s in range(SECT):
                    eng.dma_start(dst[FD * s:FD * s + FD, 8 * g:8 * g + 8, :], part[gi % 2][PARTS[gi][s]][:, :])\
                       .then_inc(s_stk[gi % 2], 16)

            def store_x1(v, bb):
                eng.wait_ge(s_x1, 2 * v + bb + 2)
                eng.dma_start(out[bass.ds((v * 2 + bb) * SEQ, SEQ), :].rearrange("(t p) d -> p t d", p=P),
                              x1[bb][:, :, :]).then_inc(s_x1o[bb], 16)

            def store_h2(v, bb):
                eng.wait_ge(s_h2, 2 * v + bb + 1)
                eng.dma_start(rows[bass.ds((v * 2 + bb) * SEQ, SEQ), 0:D].rearrange("(t p) d -> p t d", p=P),
                              h2[bb][:, :, :]).then_inc(s_h2o[bb], 16)

            for gi in range(4):
                stacks(gi, 0, gi)
            eng.wait_ge(s_gbrow, 16)
            eng.wait_ge(s_cb, 2)

            def unit(u, par, first, last):
                if not first:
                    store_x1(u - 1, 0)
                if not last:
                    stacks(4 * u + 4, 1 - par, 0)
                if not first:
                    store_h2(u - 1, 0)
                    store_x1(u - 1, 1)
                if not last:
                    stacks(4 * u + 5, 1 - par, 1)
                if not first:
                    store_h2(u - 1, 1)
                if not last:
                    stacks(4 * u + 6, 1 - par, 2)
                    stacks(4 * u + 7, 1 - par, 3)

            units(eng, unit)
            for bb in range(2):
                store_x1(UNITS - 1, bb)
                store_h2(UNITS - 1, bb)
            eng.wait_ge(s_x1, 2 * UNITS + 1)
            eng.dma_start(w1_sb, w1.rearrange("e p f -> p e f")).then_inc(s_wf, 16)
            eng.wait_ge(s_h2, 2 * UNITS)
            for e in range(NE):
                eng.dma_start(w2_sb[:, e, :, :], w2[e, :, :].rearrange("(k p) d -> p k d", p=P)).then_inc(s_wf, 16)
            eng.wait_ge(s_pte, 1)
            with nc.allow_non_contiguous_dma(reason="eight probabilities a token"):
                eng.dma_start(rows[:, 2 * D:ROW].rearrange("(t p) e -> p t e", p=P), pr_te[:, :, :]).then_inc(s_pro, 16)

        @block.gpsimd
        def _(eng):
            eng.sem_inc(s_x1, 1)
            eng.sem_inc(s_h2c, 1)
            nc.gpsimd.memset(ident[:, :], 0.0).then_inc(s_k0, 1)
            nc.gpsimd.memset(ones_f[:, :], 1.0)
            nc.gpsimd.memset(mask[:, :, :], 1.0).then_inc(s_k0, 1)
            nc.gpsimd.memset(half_neg[:, :], -0.5)
            eng.wait_ge(s_k0, 2)
            nc.gpsimd.affine_select(out=ident[:, :], in_=ident[:, :], compare_op=ALU.not_equal, fill=1.0,
                                    base=0, pattern=[[-1, P]], channel_multiplier=1)
            nc.gpsimd.affine_select(out=mask[:, :, :], in_=mask[:, :, :], compare_op=ALU.is_ge, fill=0.0, base=0,
                                    pattern=[[0, 2], [1, BK]], channel_multiplier=-1).then_inc(s_const, 1)
            for p in range(2):
                nc.gpsimd.memset(v_bd[p][:, :, :, :], 0.0)
            nc.gpsimd.memset(csum[:, :], 0.0).then_inc(s_vz, 1)
            eng.dma_start(b1_sb[:, :, :], b1.rearrange("p (e k) -> p e k", e=NE)).then_inc(s_bias, 16)
            eng.dma_start(b2_sb[:, :, :].rearrange("p e d -> p (e d)"),
                          b2.rearrange("e d -> (e d)").unsqueeze(0).broadcast_to([P, NE * D])).then_inc(s_bias, 16)

            def routing_constants():
                nc.gpsimd.memset(blk[:, :], 0.0)
                nc.gpsimd.memset(upper[:, :], 1.0)
                nc.gpsimd.memset(ones_b[:, :], 1.0)
                nc.gpsimd.memset(not_first[:, :, :], 1.0).then_inc(s_cb, 1)
                eng.wait_ge(s_cb, 1)
                nc.gpsimd.memset(not_first[:, :, 0:1], 0.0)
                nc.gpsimd.affine_select(out=upper[:, :], in_=upper[:, :], compare_op=ALU.is_gt, fill=0.0, base=0,
                                        pattern=[[1, P]], channel_multiplier=-1)
                nc.gpsimd.iota(iota_i[:, 0:1], pattern=[[0, 1]], base=0, channel_multiplier=1).then_inc(s_ci, 1)
                eng.wait_ge(s_ci, 1)
                nc.gpsimd.tensor_copy(iota_p[:, :], iota_i[:, 0:1]).then_inc(s_ci, 1)
                eng.wait_ge(s_ci, 2)
                nc.gpsimd.iota(iota_i, pattern=[[1, 32], [0, NT]], base=0, channel_multiplier=0).then_inc(s_ci, 1)
                eng.wait_ge(s_ci, 3)
                nc.gpsimd.tensor_copy(iota_v[:, :, :].rearrange("p v t -> p (v t)"), iota_i).then_inc(s_ci, 1)
                eng.wait_ge(s_ci, 4)
                nc.gpsimd.iota(iota_i[:, 0:16 * NT], pattern=[[0, 16], [1, NT]], base=0, channel_multiplier=0)\
                    .then_inc(s_ci, 1)
                eng.wait_ge(s_ci, 5)
                nc.gpsimd.tensor_copy(iota_t[:, :, :].rearrange("p v t -> p (v t)"), iota_i[:, 0:16 * NT])\
                    .then_inc(s_cb, 1)

            def rstd(n, s_mo, s_ve, s_rs, mom, vare, rs):
                cols = vare.shape[1]
                eng.wait_ge(s_mo, n + 1)
                alone(eng)
                nc.gpsimd.tensor_scalar(vare, mom[:, :, 1], EPS_LN, None, ALU.add).then_inc(s_ve, 1)
                eng.wait_ge(s_ve, n + 1)
                nc.gpsimd.tensor_tensor(rs, vare, half_neg[:, 0:cols], ALU.pow).then_inc(s_rs, 1)

            def rstd1_of(n):
                t0, t1 = (0, UT) if n == 0 else (UT, NT)
                rstd(n, s_mo1, s_ve1, s_rs1, mom1[:, t0:t1, :], vare1[:, t0:t1], rstd1[:, t0:t1])

            def rstd2_of(v, bb):
                rstd(2 * v + bb, s_mo2, s_ve2, s_rs2, mom2, vare2[:, :], rstd2[:, :])

            def low_part(n, buf):
                eng.wait_ge(s_p2, n + 1)
                nc.gpsimd.tensor_tensor(part[buf][2][:, :], resid[buf][:, :], part[buf][1][:, :], ALU.subtract)\
                    .then_inc(s_p3, 1)

            def residual_add(v, bb):
                eng.wait_ge(s_x1o[bb], 16 * v + 16)
                eng.wait_ge(s_ga, 2 * v + bb + 1)
                t0 = v * UT + 2 * bb
                nc.gpsimd.tensor_tensor(x1[bb][:, :, :], gated[:, :, :], xall[:, bass.ds(t0, 2), :], ALU.add)\
                    .then_inc(s_x1, 1)

            def modulate2(v, bb):
                eng.wait_ge(s_h2o[bb], 16 * v + 16)
                n = 2 * v + bb
                eng.wait_ge(s_xn2, n + 1)
                b = v * 2 + bb
                nc.gpsimd.tensor_tensor(h2c[:, :, :], xn2[:, :, :],
                                        cb_sb[:, bass.ds(b, 1), :].broadcast_to([P, 2, D]), ALU.mult).then_inc(s_h2c, 1)
                eng.wait_ge(s_h2c, n + 2)
                nc.gpsimd.tensor_tensor(h2[bb][:, :, :], h2c[:, :, :],
                                        sb_sb[:, bass.ds(b, 1), :].broadcast_to([P, 2, D]), ALU.add).then_inc(s_h2, 1)

            rstd1_of(0)
            for gi in range(4):
                low_part(gi, gi % 2)
            rstd1_of(1)
            eng.wait_ge(s_mod[9], 1)
            eng.dma_start(rows[:, D:2 * D].rearrange("(b n) d -> b n d", b=NB),
                          modout[:, 3, :].unsqueeze(1).broadcast_to([NB, SEQ, D])).then_inc(s_gbrow, 16)
            routing_constants()
            eng.wait_ge(s_bc, 48)
            eng.wait_ge(s_x, 16 * NX)

            def unit(u, par, first, last):
                if not first:
                    low_part(4 * u + 3, 1)
                    residual_add(u - 1, 0)
                if not last:
                    low_part(4 * u + 4, 0)
                if not first:
                    rstd2_of(u - 1, 0)
                    modulate2(u - 1, 0)
                    residual_add(u - 1, 1)
                if not last:
                    low_part(4 * u + 5, 1)
                if not first:
                    rstd2_of(u - 1, 1)
                    modulate2(u - 1, 1)
                if not last:
                    low_part(4 * u + 6, 0)

            units(eng, unit)
            for bb in range(2):
                residual_add(UNITS - 1, bb)
                rstd2_of(UNITS - 1, bb)
                modulate2(UNITS - 1, bb)

            def gather(e):
                eng.wait_ge(s_idx, e + 1)
                if e >= 4:
                    eng.wait_ge(s_o, e - 3)
                for j in range(CT):
                    eng.indirect_dma_start(out=xg[e % 4][:, j, :], out_offset=None, in_=rows[:, :],
                                           in_offset=bass.IndirectOffsetOnAxis(ap=idx[:, e, j:j + 1].bitcast(u32), axis=0))\
                       .then_inc(s_xg[e % 4], 16)

            def scatter(e):
                eng.wait_ge(s_o, e + 1)
                if e:
                    eng.wait_ge(s_sc, 16 * CT * e)
                for j in range(CT):
                    eng.indirect_dma_start(out=out[:, :],
                                           out_offset=bass.IndirectOffsetOnAxis(ap=idx[:, e, j:j + 1].bitcast(u32), axis=0),
                                           in_=o_sb[e % 2][:, j, :], in_offset=None, compute_op=ALU.add)\
                       .then_inc(s_sc, 16)

            for bb in range(2):
                eng.wait_ge(s_x1o[bb], 16 * UNITS + 16)
                eng.wait_ge(s_h2o[bb], 16 * UNITS + 16)
            eng.wait_ge(s_gbrow, 16)
            eng.wait_ge(s_pro, 16)
            for e in range(3):
                gather(e)
            for e in range(NE):
                if e + 3 < NE:
                    gather(e + 3)
                scatter(e)
            eng.wait_ge(s_sc, 16 * CT * NE)

        @block.scalar
        def _(eng):
            eng.wait_ge(s_c, 16)
            nc.scalar.activation(c_exp[:, :], c_sb[:, :], ACT.Exp, scale=-1.0).then_inc(s_mod[0], 1)

            def high_part_of(u, gi):
                n = 4 * u + gi
                wait(eng, s_stk[gi % 2], (u * 2 + gi // 2) * 16 * SECT)
                eng.wait_ge(s_qkp, n + 1)
                nc.scalar.activation(part[gi % 2][0][:, :], ps[:, B_FR, :], ACT.Copy).then_inc(s_p1, 1)

            def middle_part(n, buf):
                eng.wait_ge(s_re, n + 1)
                nc.scalar.activation(part[buf][1][:, :], resid[buf][:, :], ACT.Copy).then_inc(s_p2, 1)

            def modulate1(u):
                eng.wait_ge(s_htp, u + 1)
                for bb in range(2):
                    b = u * 2 + bb
                    k = nc.scalar.activation(h_t[:, bb * SEQ:(bb + 1) * SEQ], ps[:, B_FR, bb * SEQ:(bb + 1) * SEQ],
                                             ACT.Identity, scale=ca_t[:, bass.ds(b, 1)], bias=sa_t[:, bass.ds(b, 1)])
                k.then_inc(s_ht, 1)

            def v_even(u, par):
                eng.wait_ge(s_vp, u + 1)
                nc.scalar.activation(v_bd[par][0:BK, :, :, 0:HD].rearrange("p j r d -> p (j r) d"),
                                     ps[0:BK, B_FR, :].rearrange("p (a d) -> p a d", d=HD), ACT.Copy).then_inc(s_va, 1)

            def square(Q, sp, half):
                eng.wait_ge(s_scA, 2 * Q + half + 1)
                wait(eng, s_pv, Q - 1)
                nc.scalar.activation(wgt[sp][:, 2 * half:2 * half + 2, :], ps[:, 2 * half:2 * half + 2, :],
                                     ACT.Square, scale=0.25, bias=1.0).then_inc(s_sqA, 1)

            def square2(Q, sp):
                eng.wait_ge(s_scB, Q + 1)
                nc.scalar.activation(wgt2[sp][:, :, :], ps[:, B_S2, :].rearrange("p (c q) -> p c q", c=4),
                                     ACT.Square, scale=0.25, bias=1.0).then_inc(s_sqB, 1)

            def y_copy(v, bb):
                eng.wait_ge(s_ydp, 2 * v + bb + 1)
                nc.scalar.activation(y_d[:, :], ps[:, B_PO, 0:SEQ], ACT.Copy).then_inc(s_yd, 1)

            def h2_copy(v, bb):
                eng.wait_ge(s_h2p, 2 * v + bb + 1)
                nc.scalar.activation(h2_t[:, :], ps[:, B_PO, 0:SEQ], ACT.Copy).then_inc(s_h2t, 1)

            eng.wait_ge(s_mod[11], 1)
            modulate1(0)
            for gi in range(2):
                high_part_of(0, gi)
                middle_part(gi, gi % 2)
            eng.wait_ge(s_vinit, 1)
            v_even(0, 0)
            for gi in range(2, 4):
                high_part_of(0, gi)
                middle_part(gi, gi % 2)

            def unit(u, par, first, last):
                for s in range(4):
                    Q = u * 4 + s
                    square(Q, s % 2, 0)
                    if (s == 0 and not first) or (s > 0 and not last):
                        middle_part(4 * u + s + 3, (s + 1) % 2)
                    if s >= 2 and not first:
                        h2_copy(u - 1, s - 2)
                    if s == 2 and not last:
                        v_even(u + 1, 1 - par)
                    square(Q, s % 2, 1)
                    square2(Q, s % 2)
                    if s < 2 and not first:
                        y_copy(u - 1, s)
                    if s == 0 and not last:
                        modulate1(u + 1)
                    if not last:
                        high_part_of(u + 1, s)

            units(eng, unit)
            for bb in range(2):
                y_copy(UNITS - 1, bb)
            for bb in range(2):
                h2_copy(UNITS - 1, bb)
            eng.wait_ge(s_cb, 2)
            eng.wait_ge(s_sh, 1)
            nc.scalar.activation(ex[:, :, :], sh[:, :, :], ACT.Exp).then_inc(s_ex, 1)
            eng.wait_ge(s_pr, 1)
            nc.scalar.activation(pr_te[:, :, :].rearrange("p t e -> p e t"), pr[:, :, :], ACT.Copy).then_inc(s_pte, 1)
            for e in range(NE):
                eng.wait_ge(s_ohh, e + 1)
                nc.scalar.activation(oh_hi[:, e, 0, :, :].rearrange("p v t -> p (v t)"),
                                     oh_hi[:, e, 1, :, :].rearrange("p v t -> p (v t)"), ACT.Copy,
                                     scale=iota_p[:, 0:1]).then_inc(s_ohp, 1)
            for g in range(2):
                eng.wait_ge(s_ixp, g + 1)
                nc.scalar.activation(idx_p[:, 4 * g:4 * g + 4, :],
                                     ps[:, 4 + g, 0:P].rearrange("p (e a v) -> p e a v", e=4, a=2)[:, :, 0, :],
                                     ACT.Copy).then_inc(s_ixc, 1)
            eng.wait_ge(s_bias, 32)
            for e in range(NE):
                for k in range(FC):
                    eng.wait_ge(s_h1, FC * e + k + 1)
                    nc.scalar.activation(g_sb[:, k, :], ps[:, k, :], ACT.Gelu_apprx_tanh, bias=b1_sb[:, e, k:k + 1])\
                        .then_inc(s_g, 1)

        @block.vector
        def _(eng):
            eng.sem_inc(s_lg, 1)
            eng.wait_ge(s_mod[0], 1)
            nc.vector.tensor_scalar(c_den[:, :], c_exp[:, :], 1.0, None, ALU.add).then_inc(s_mod[1], 1)
            eng.wait_ge(s_mod[1], 1)
            nc.vector.reciprocal(c_sig[:, :], c_den[:, :]).then_inc(s_mod[2], 1)
            eng.wait_ge(s_mod[2], 1)
            nc.vector.tensor_tensor(c_silu[:, :], c_sb[:, :], c_sig[:, :], ALU.mult).then_inc(s_mod[3], 1)

            def moments1(n, t0, t1):
                for t in range(t0, t1):
                    k = nc.vector.bn_stats(stats1[:, t, :], xall[:, t, :])
                k.then_inc(s_st1, 1)
                eng.wait_ge(s_st1, n + 1)
                alone(eng)
                for t in range(t0, t1):
                    k = nc.vector.bn_aggr(mom1[:, t, :], stats1[:, t, :])
                k.then_inc(s_mo1, 1)

            def normalise1(u):
                eng.wait_ge(s_rs1, 1 if isinstance(u, int) and u == 0 else 2)
                wait(eng, s_htp, u)
                for t in range(UT):
                    k = nc.vector.tensor_scalar(xn1[:, t, :],
                                                xall[:, bass.ds(u * UT + t, 1), :].rearrange("p o d -> p (o d)"),
                                                mom1[:, bass.ds(u * UT + t, 1), 0:1].rearrange("p o d -> p (o d)"),
                                                rstd1[:, bass.ds(u * UT + t, 1)], ALU.subtract, ALU.mult)
                k.then_inc(s_xn1, 1)

            def residual(n, buf):
                eng.wait_ge(s_p1, n + 1)
                wait(eng, s_p3, n - 1)
                nc.vector.tensor_tensor(resid[buf][:, :], ps[:, B_FR, :], part[buf][0][:, :], ALU.subtract)\
                    .then_inc(s_re, 1)

            def v_odd(u, par):
                eng.wait_ge(s_vp, u + 1)
                nc.vector.tensor_copy(v_bd[par][BK:P, :, :, HD + 1:2 * HD + 1].rearrange("p j r d -> p (j r) d"),
                                      ps[BK:P, B_FR, :].rearrange("p (a d) -> p a d", d=HD)).then_inc(s_vb, 1)

            def mask_half(Q, sp, half):
                eng.wait_ge(s_sqA, 2 * Q + half + 1)
                w = wgt[sp][:, 2 * half:2 * half + 2, :]
                m2 = mask[:, :, :].rearrange("p a q -> p (a q)").unsqueeze(1).broadcast_to([P, 2, 2 * BK])
                m1 = mask[:, 0:1, :].broadcast_to([P, 2, BK])
                d = w[:, :, COL3:COL3 + 2 * BK]
                nc.vector.scalar_tensor_tensor(d, d, 1.0, m2, ALU.add, ALU.mult)
                d = w[:, :, COL1:COL1 + BK]
                nc.vector.scalar_tensor_tensor(d, d, 1.0, m1, ALU.add, ALU.mult).then_inc(s_mk, 1)

            def mask_2(Q, sp):
                eng.wait_ge(s_sqB, Q + 1)
                d = wgt2[sp][:, :, 0:BK]
                nc.vector.scalar_tensor_tensor(d, d, 1.0, mask[:, 0:1, :].broadcast_to([P, 4, BK]), ALU.add, ALU.mult)\
                    .then_inc(s_mk, 1)

            def y_out(Q, bb, qd):
                eng.wait_ge(s_pv, Q + 1)
                nc.vector.tensor_copy(csum[:, 1:4], ps[:, B_PV, SEQ:SEQ + 3]).then_inc(s_cs, 1)
                eng.wait_ge(s_cs, Q + 1)
                nc.vector.tensor_tensor(y_t[:, bb, qd, :].rearrange("p (i q) -> p i q", i=4),
                                        ps[:, B_PV, 0:SEQ].rearrange("p (i q) -> p i q", i=4),
                                        csum[:, :].unsqueeze(2).broadcast_to([P, 4, BK]), ALU.add).then_inc(s_yt, 1)

            def y_norm(v, bb):
                n = 2 * v + bb
                tok = ps[:, B_PO, :].rearrange("p (g r) -> p g r", g=16)
                eng.wait_ge(s_ya, n + 1)
                nc.vector.tensor_scalar(den[:, :, :], tok[:, :, HD:2 * HD + 2:HD + 1], EPS_DEN, None, ALU.add)\
                    .then_inc(s_den, 1)
                eng.wait_ge(s_den, n + 1)
                nc.vector.reciprocal(rec[:, :, :], den[:, :, :]).then_inc(s_rec, 1)
                eng.wait_ge(s_rec, n + 1)
                nc.vector.tensor_tensor(y_tok[:, :, :].rearrange("p t (g a d) -> p (t g) a d", a=2, d=HD),
                                        tok[:, :, 0:2 * HD + 2].rearrange("p g (a d) -> p g a d", a=2)[:, :, :, 0:HD],
                                        rec[:, :, :].unsqueeze(3).broadcast_to([P, 16, 2, HD]), ALU.mult)\
                    .then_inc(s_yn, 1)

            def gate(v, bb):
                eng.wait_ge(s_at, 2 * v + bb + 1)
                eng.wait_ge(s_x1, 2 * v + bb + 1)
                nc.vector.tensor_tensor(gated[:, :, :], ps[:, B_PO, SEQ:2 * SEQ].rearrange("p (t d) -> p t d", t=2),
                                        ga_sb[:, bass.ds(v * 2 + bb, 1), :].broadcast_to([P, 2, D]), ALU.mult)\
                    .then_inc(s_ga, 1)

            def moments2(v, bb):
                n = 2 * v + bb
                eng.wait_ge(s_x1, n + 2)
                for t in range(2):
                    k = nc.vector.bn_stats(stats2[:, t, :], x1[bb][:, t, :])
                k.then_inc(s_st2, 1)
                eng.wait_ge(s_st2, n + 1)
                alone(eng)
                for t in range(2):
                    k = nc.vector.bn_aggr(mom2[:, t, :], stats2[:, t, :])
                k.then_inc(s_mo2, 1)

            def normalise2(v, bb):
                n = 2 * v + bb
                eng.wait_ge(s_rs2, n + 1)
                eng.wait_ge(s_h2c, n + 1)
                for t in range(2):
                    k = nc.vector.tensor_scalar(xn2[:, t, :], x1[bb][:, t, :], mom2[:, t, 0:1], rstd2[:, t:t + 1],
                                                ALU.subtract, ALU.mult)
                k.then_inc(s_xn2, 1)

            def logits(v, bb):
                eng.wait_ge(s_lgp, 2 * v + bb + 1)
                nc.vector.tensor_tensor(lg[:, :, bass.ds(v * UT + 2 * bb, 2)],
                                        ps[:, B_PO, SEQ:SEQ + 2 * NE].rearrange("p (t e) -> p e t", t=2),
                                        bs_sb[:, :].unsqueeze(2).broadcast_to([P, NE, 2]), ALU.add).then_inc(s_lg, 1)

            eng.wait_ge(s_x, 16)
            moments1(0, 0, UT)
            eng.wait_ge(s_const, 1)
            nc.vector.tensor_copy(mask[BK:P, :, :], mask[0:BK, :, :])
            eng.wait_ge(s_mod[4], 1)
            nc.vector.tensor_copy(c_t[:, :], ps[:, 0, 0:NB]).then_inc(s_mod[5], 1)
            eng.wait_ge(s_mod[6], 1)
            nc.vector.tensor_scalar(ca_t[:, :], ps[:, 3, 0:NB], 1.0, None, ALU.add)
            nc.vector.tensor_copy(sa_t[:, :], ps[:, 3, NB:2 * NB]).then_inc(s_mod[11], 1)
            normalise1(0)
            eng.wait_ge(s_vz, 1)
            for p in range(2):
                nc.vector.memset(v_bd[p][0:BK, :, :, HD:HD + 1], 1.0)
                k = nc.vector.memset(v_bd[p][BK:P, :, :, 2 * HD + 1:2 * HD + 2], 1.0)
            k.then_inc(s_vinit, 1)
            nc.vector.tensor_copy(mod_sb[:, :, :].rearrange("b n d -> b (n d)")[:, 0:512], ps[0:NB, 1, :])
            nc.vector.tensor_copy(mod_sb[:, :, :].rearrange("b n d -> b (n d)")[:, 512:768], ps[0:NB, 2, 0:256])\
                .then_inc(s_mod[7], 1)
            eng.wait_ge(s_mod[7], 1)
            g = mod_sb[:, 2:6:3, :]
            nc.vector.tensor_scalar(g_sign[:, :, :], g, 0.0, 2.0, ALU.is_ge, ALU.mult)
            nc.vector.scalar_tensor_tensor(g_mag[:, :, :], g, -1.0, g, ALU.mult, ALU.max).then_inc(s_mod[8], 1)
            eng.wait_ge(s_mod[8], 1)
            nc.vector.tensor_scalar(g_mag[:, :, :], g_mag[:, :, :], 0.25, None, ALU.max).then_inc(s_mod[8], 1)
            eng.wait_ge(s_mod[8], 2)
            nc.vector.scalar_tensor_tensor(modout[:, 0:4:3, :], g_sign[:, :, :], 1.0, g_mag[:, :, :],
                                           ALU.subtract, ALU.mult)
            nc.vector.tensor_scalar(modout[:, 1, :], mod_sb[:, 4, :], 1.0, None, ALU.add)
            nc.vector.tensor_copy(modout[:, 2, :], mod_sb[:, 3, :]).then_inc(s_mod[9], 1)
            for gi in range(2):
                residual(gi, gi % 2)
            eng.wait_ge(s_vinit, 1)
            v_odd(0, 0)
            eng.wait_ge(s_x, 16 * NX)
            moments1(1, UT, NT)
            for gi in range(2, 4):
                residual(gi, gi % 2)
            eng.wait_ge(s_bc, 48)

            def unit(u, par, first, last):
                for s in range(4):
                    Q = u * 4 + s
                    if s == 0 and not last:
                        normalise1(u + 1)
                    mask_half(Q, s % 2, 0)
                    if s < 2 and not first:
                        y_norm(u - 1, s)
                    if s in (1, 2) and not first:
                        moments2(u - 1, s - 1)
                    if s == 2 and not last:
                        v_odd(u + 1, 1 - par)
                    mask_half(Q, s % 2, 1)
                    mask_2(Q, s % 2)
                    if s >= 2 and not first:
                        logits(u - 1, s - 2)
                    if s in (1, 2) and not first:
                        normalise2(u - 1, s - 1)
                    if not (first and s == 0):
                        y_out(Q - 1, (s - 1) % 2, ((s - 1) % 4) // 2)
                    if s < 2 and not first:
                        gate(u - 1, s)
                    if not last:
                        residual(4 * u + 4 + s, s % 2)

            units(eng, unit)
            eng.wait_ge(s_cb, 1)
            for q in range(4):
                k = nc.vector.memset(blk[32 * q:32 * q + 32, 32 * q:32 * q + 32], 1.0)
            k.then_inc(s_blk, 1)
            v = UNITS - 1
            y_norm(v, 0)
            y_out(4 * UNITS - 1, 1, 1)
            gate(v, 0)
            y_norm(v, 1)
            moments2(v, 0)
            gate(v, 1)
            normalise2(v, 0)
            moments2(v, 1)
            logits(v, 0)
            normalise2(v, 1)
            logits(v, 1)

            done = [0]

            def link(ins):
                done[0] += 1
                ins.then_inc(s_r, 1)
                eng.wait_ge(s_r, done[0])

            eng.wait_ge(s_lg, 2 * UNITS + 1)
            link(nc.vector.tensor_reduce(mx[:, :], lg[:, :, :].rearrange("p e t -> p t e"), AX.X, ALU.max))
            nc.vector.tensor_tensor(sh[:, :, :], lg[:, :, :], mx[:, :].unsqueeze(1).broadcast_to([P, NE, NT]),
                                    ALU.subtract).then_inc(s_sh, 1)
            eng.wait_ge(s_ex, 1)
            link(nc.vector.tensor_reduce(sm[:, :], ex[:, :, :].rearrange("p e t -> p t e"), AX.X, ALU.add))
            link(nc.vector.reciprocal(rsm[:, :], sm[:, :]))
            nc.vector.tensor_tensor(pr[:, :, :], ex[:, :, :], rsm[:, :].unsqueeze(1).broadcast_to([P, NE, NT]),
                                    ALU.mult).then_inc(s_pr, 1)
            nc.vector.memset(cand[:, :], 2.0 ** -63)
            eng.wait_ge(s_ptp, 1)
            link(nc.vector.tensor_copy(p_t[:, :, :], ps[:, 0, 0:2 * P].rearrange("p (h q) -> p h q", h=2)))

            def compare():
                for h in range(2):
                    k = nc.vector.tensor_scalar(hit[:, h, :], p_t[:, h, :], cand[:, h:h + 1], 0.0, ALU.is_ge, ALU.add,
                                                accum_out=cnt[:, h:h + 1])
                k.then_inc(s_cmp, 1)

            total = ps[:, 1, 0:2]
            for n, s in enumerate(EXP_STEPS):
                up, down = 2.0 ** s, 2.0 ** -s
                compare()
                eng.wait_ge(s_cnt, n + 1)
                link(nc.vector.tensor_scalar(upd[:, :], total, float(CAP), up - down, ALU.is_ge, ALU.mult))
                link(nc.vector.scalar_tensor_tensor(cand[:, :], upd[:, :], down, cand[:, :], ALU.add, ALU.mult))
            NEXP = len(EXP_STEPS) + 1
            compare()
            eng.wait_ge(s_cnt, NEXP)
            link(nc.vector.tensor_scalar(upd[:, :], total, float(CAP), 0.5, ALU.is_ge, ALU.mult))
            link(nc.vector.scalar_tensor_tensor(cand_low[:, :], upd[:, :], 0.5, cand[:, :], ALU.add, ALU.mult))
            for k in range(3):
                nc.vector.tensor_scalar(steps[:, :, k], cand_low[:, :], ((k + 1) / 4 - 1) / 2, None, ALU.mult)
                nc.vector.tensor_scalar(cand3[:, :, k], cand_low[:, :], 1 + (k + 1) / 2, None, ALU.mult)
            link(nc.vector.tensor_scalar(steps[:, :, 3], cand_low[:, :], 0.5, None, ALU.mult))

            def compare3():
                for h in range(2):
                    for c in range(3):
                        k = nc.vector.tensor_scalar(hit[:, 3 * h + c, :], p_t[:, h, :], cand3[:, h, c:c + 1], 0.0,
                                                    ALU.is_ge, ALU.add, accum_out=cnt[:, 3 * h + c:3 * h + c + 1])
                k.then_inc(s_cmp, 1)

            def count_reached():
                for h in range(2):
                    k = nc.vector.tensor_scalar(reached[:, h, :], ps[:, 1, 3 * h:3 * h + 3], float(CAP), 0.0,
                                                ALU.is_ge, ALU.add, accum_out=steps_up[:, h:h + 1])
                return k

            with eng.Fori(0, QUARTERINGS - 1) as i:
                compare3()
                nc.vector.tensor_tensor(next3[:, :, :], cand3[:, :, 0:1].broadcast_to([P, 2, 3]), steps[:, :, 0:3],
                                        ALU.add)
                nc.vector.tensor_scalar(next_steps[:, :, :], steps[:, :, :], 0.25, None, ALU.mult).then_inc(s_nxt, 1)
                eng.wait_ge(s_cnt, NEXP + 1 + i)
                count_reached().then_inc(s_upd, 1)
                eng.wait_ge(s_nxt, i + 1)
                eng.wait_ge(s_upd, i + 1)
                for h in range(2):
                    k = nc.vector.scalar_tensor_tensor(cand3[:, h, :], steps[:, h, 3:4].broadcast_to([P, 3]),
                                                       steps_up[:, h:h + 1], next3[:, h, :], ALU.mult, ALU.add)
                k.then_inc(s_cand, 1)
                eng.wait_ge(s_cand, 2 * i + 1)
                nc.vector.tensor_copy(steps[:, :, :], next_steps[:, :, :]).then_inc(s_cand, 1)
                eng.wait_ge(s_cand, 2 * i + 2)
            compare3()
            link(nc.vector.tensor_tensor(cand_low[:, :], cand3[:, :, 0], steps[:, :, 3], ALU.subtract))
            eng.wait_ge(s_cnt, NEXP + QUARTERINGS)
            link(count_reached())
            link(nc.vector.tensor_tensor(upd[:, :], steps_up[:, :], steps[:, :, 3], ALU.mult))
            link(nc.vector.tensor_tensor(cand[:, :], cand_low[:, :], upd[:, :], ALU.add))
            sel = ident[:, 0:P:32]
            nc.vector.tensor_tensor(thr_d[:, :, :], sel.unsqueeze(1).broadcast_to([P, 2, 4]),
                                    cand[:, :].unsqueeze(2).broadcast_to([P, 2, 4]), ALU.mult).then_inc(s_td, 1)
            eng.wait_ge(s_thp, 1)
            link(nc.vector.tensor_copy(thr[:, :], ps[:, 1, 8:8 + NE]))
            thr_b = thr[:, :].unsqueeze(2).broadcast_to([P, NE, NT])
            nc.vector.tensor_tensor(pick[:, 0, :, :], pr[:, :, :], thr_b, ALU.is_gt)
            link(nc.vector.tensor_tensor(pick[:, 1, :, :], pr[:, :, :], thr_b, ALU.is_equal))
            eng.wait_ge(s_cb, 2)
            flat = lambda a: a[:, :, :, :].rearrange("p a e t -> p (a e t)")
            link(nc.vector.tensor_tensor_scan(flat(seen), not_first[:, :, :].rearrange("p g t -> p (g t)"), flat(pick),
                                              0.0, ALU.mult, ALU.add))
            nc.vector.tensor_tensor(flat(seen_x), flat(seen), flat(pick), ALU.subtract).then_inc(s_seen, 1)
            eng.wait_ge(s_posp, 1)
            nc.vector.tensor_copy(cgt[:, :], ps[:, 3, 0:NE])
            link(nc.vector.scalar_tensor_tensor(flat(pos), flat(pick), -float(NTOK), ps[:, 2, :], ALU.mult, ALU.add))
            link(nc.vector.tensor_tensor(pos[:, 1, :, :], pos[:, 1, :, :],
                                         cgt[:, :].unsqueeze(2).broadcast_to([P, NE, NT]), ALU.add))
            link(nc.vector.tensor_tensor(pos_m[:, :, :], pos[:, 0, :, :], pos[:, 1, :, :], ALU.min))
            link(nc.vector.tensor_scalar(pos_i[:, :, :], pos_m[:, :, :], float(NTOK), None, ALU.add))
            nc.vector.tensor_scalar(lo_i[:, :, :], pos_i[:, :, :], 31, None, ALU.bitwise_and)
            link(nc.vector.tensor_scalar(hi_i[:, :, :], pos_i[:, :, :], 5, None, ALU.logical_shift_right))
            nc.vector.tensor_copy(lo_b[:, :, :], lo_i[:, :, :])
            link(nc.vector.tensor_copy(hi_b[:, :, :], hi_i[:, :, :]))
            for e in range(NE):
                nc.vector.tensor_tensor(oh_hi[:, e, 1, :, :], hi_b[:, e, :].unsqueeze(1).broadcast_to([P, 16, NT]),
                                        iota_v[:, 0:16, :], ALU.is_equal).then_inc(s_ohh, 1)
                nc.vector.tensor_tensor(oh_lo[:, e, :, :], lo_b[:, e, :].unsqueeze(1).broadcast_to([P, 32, NT]),
                                        iota_v[:, :, :], ALU.is_equal)
                eng.wait_ge(s_ohp, e + 1)
                nc.vector.tensor_tensor(oh_hi[:, e, 1, :, :], oh_hi[:, e, 1, :, :], iota_t[:, :, :], ALU.mult)\
                    .then_inc(s_oh, 1)
            for g in range(2):
                eng.wait_ge(s_ixc, g + 1)
                link(nc.vector.scalar_tensor_tensor(
                    idx_s[:, 4 * g:4 * g + 4, :],
                    ps[:, 4 + g, 0:P].rearrange("p (e a v) -> p e a v", e=4, a=2)[:, :, 1, :], float(P),
                    idx_p[:, 4 * g:4 * g + 4, :], ALU.mult, ALU.add))
                for e in range(4 * g, 4 * g + 4):
                    for cc in range(4):
                        q = 32 * (e % 4)
                        k = nc.vector.tensor_copy(idx[32 * cc:32 * cc + 32, e, :],
                                                  idx_s[q:q + 32, e, CT * cc:CT * cc + CT])
                    k.then_inc(s_idx, 1)

            def x_copy(e):
                eng.wait_ge(s_xtp, e + 1)
                nc.vector.tensor_copy(x_t[e % 2], ps[:, 6 + e % 2, :]).then_inc(s_xt, 1)

            eng.wait_ge(s_bias, 32)
            x_copy(0)
            for e in range(NE):
                if e + 1 < NE:
                    x_copy(e + 1)
                eng.wait_ge(s_op, e + 1)
                if e:
                    eng.wait_ge(s_o, e)
                nc.vector.tensor_tensor(o_b[:, :, :], ps[:, 4 + e % 2, :].rearrange("p (j d) -> p j d", j=CT),
                                        b2_sb[:, e:e + 1, :].broadcast_to([P, CT, D]), ALU.add).then_inc(s_ob, 1)
                eng.wait_ge(s_ob, e + 1)
                if e >= 2:
                    eng.wait_ge(s_sc, 16 * CT * (e - 1))
                g = xg[e % 4]
                for j in range(CT):
                    k = nc.vector.scalar_tensor_tensor(o_sb[e % 2][:, j, :], o_b[:, j, :],
                                                       g[:, j, 2 * D + e:2 * D + e + 1], g[:, j, D:2 * D],
                                                       ALU.mult, ALU.mult)
                k.then_inc(s_o, 1)

        @block.tensor
        def _(eng):
            mm = nc.tensor.matmul
            tr = nc.tensor.transpose

            def to_h_t(u):
                eng.wait_ge(s_xn1, u + 1)
                wait(eng, s_re, 4 * u)
                for t in range(UT):
                    k = tr(ps[:, B_FR, t * P:(t + 1) * P], xn1[:, t, :], ident[:, :])
                k.then_inc(s_htp, 1)

            def project(u, gi):
                eng.wait_ge(s_ht, u + 1)
                wait(eng, s_re, 4 * u + gi)
                if gi == 2:
                    eng.wait_ge(s_va, u + 1)
                    eng.wait_ge(s_vb, u + 1)
                mm(ps[:, B_FR, :], wqk_sb[:, gi, :], h_t[:, :], start=True, stop=True).then_inc(s_qkp, 1)

            def project_v(u):
                eng.wait_ge(s_re, 4 * u + 2)
                for j in range(UTOK // BK):
                    for hh in range(2):
                        k = mm(ps[BK * hh:BK * hh + BK, B_FR, j * BK:(j + 1) * BK], h_t[:, j * BK:(j + 1) * BK],
                               wv_sb[:, hh, :], start=True, stop=True)
                k.then_inc(s_vp, 1)

            def scores(Q, par, bb, pair, key, bank, col):
                t0 = bb * SEQ
                for hh in range(2):
                    head = 2 * pair + hh
                    k = mm(ps[BK * hh:BK * hh + BK, bank, col:col + SEQ - key * BK],
                           ks[par][:, head, t0 + key * BK:t0 + (key + 1) * BK],
                           qs[par][:, head, t0 + key * BK:t0 + SEQ], start=True, stop=True)
                return k

            def scores_half(Q, par, bb, qd, half):
                wait(eng, s_sqA, 2 * Q + half - 1)
                for cc in range(2 * half, 2 * half + 2):
                    for key, col in ((3, COL3), (0, COL0), (1, COL1)):
                        k = scores(Q, par, bb, 4 * qd + cc, key, cc, col)
                k.then_inc(s_scA, 1)

            def scores_2(Q, par, bb, qd):
                wait(eng, s_sqB, Q)
                for cc in range(4):
                    k = scores(Q, par, bb, 4 * qd + cc, 2, B_S2, cc * 2 * BK)
                k.then_inc(s_scB, 1)

            def weighted(Q, par, sp, bb, qd):
                wait(eng, s_yt, Q)
                eng.wait_ge(s_mk, 3 * Q + 3)
                blocks = [wgt[sp][:, :, COL0:COL0 + 256], wgt[sp][:, :, COL1:COL1 + 192],
                          wgt2[sp][:, :, :], wgt[sp][:, :, COL3:COL3 + 64]]
                for j in range(4):
                    for cc in range(4):
                        mm(ps[32 * cc:32 * cc + 32, B_PV, j * BK:SEQ], v_bd[par][:, 4 * bb + j, 4 * qd + cc, :],
                           blocks[j][:, cc, :], start=(j == 0), stop=(j == 3), skip_group_check=True)
                for j in range(3):
                    k = mm(ps[:, B_PV, SEQ + j:SEQ + 3],
                           v_bd[par][:, 4 * bb + j, 4 * qd:4 * qd + 4, :].rearrange("p r d -> p (r d)"),
                           ones_f[:, 0:3 - j], start=False, stop=(j == 2), skip_group_check=True)
                k.then_inc(s_pv, 1)

            def to_y_token(v, bb):
                eng.wait_ge(s_yt, 4 * v + 3 + bb)
                eng.wait_ge(s_lg, 2 * v + 1)
                if bb:
                    eng.wait_ge(s_ga, 2 * v + 1)
                for t in range(2):
                    for qd in range(2):
                        k = tr(ps[:, B_PO, (2 * t + qd) * P:(2 * t + qd + 1) * P], y_t[:, bb, qd, t * P:(t + 1) * P],
                               ident[:, :])
                k.then_inc(s_ya, 1)

            def to_y_d(v, bb):
                eng.wait_ge(s_yn, 2 * v + bb + 1)
                for t in range(2):
                    k = tr(ps[:, B_PO, t * P:(t + 1) * P], y_tok[:, t, :], ident[:, :])
                k.then_inc(s_ydp, 1)

            def project_out(v, bb):
                eng.wait_ge(s_yd, 2 * v + bb + 1)
                for t in range(2):
                    k = mm(ps[:, B_PO, SEQ + t * P:SEQ + (t + 1) * P], y_d[:, t * P:(t + 1) * P], wo_sb[:, :],
                           start=True, stop=True)
                k.then_inc(s_at, 1)

            def to_h2_t(v, bb, ga_count):
                eng.wait_ge(s_h2, 2 * v + bb + 1)
                eng.wait_ge(s_ga, ga_count)
                if bb:
                    eng.wait_ge(s_lg, 2 * v + 2)
                for t in range(2):
                    k = tr(ps[:, B_PO, t * P:(t + 1) * P], h2[bb][:, t, :], ident[:, :])
                k.then_inc(s_h2p, 1)

            def route(v, bb):
                eng.wait_ge(s_h2t, 2 * v + bb + 1)
                for t in range(2):
                    k = mm(ps[:, B_PO, SEQ + t * NE:SEQ + (t + 1) * NE], h2_t[:, t * P:(t + 1) * P], ws_sb[:, :],
                           start=True, stop=True)
                k.then_inc(s_lgp, 1)

            eng.wait_ge(s_const, 1)
            eng.wait_ge(s_mod[3], 1)
            tr(ps[:, 0, 0:NB], c_silu[:, :], ident[0:NB, 0:NB]).then_inc(s_mod[4], 1)
            eng.wait_ge(s_mod[5], 1)
            eng.wait_ge(s_mod[10], 16)
            mm(ps[:, 3, 0:NB], wmod_sb[:, D:2 * D], c_t[:, :], start=True, stop=True)
            mm(ps[:, 3, NB:2 * NB], wmod_sb[:, 0:D], c_t[:, :], start=True, stop=True)
            mm(ps[0:NB, 1, :], c_t[:, :], wmod_sb[:, 0:512], start=True, stop=True)
            mm(ps[0:NB, 2, 0:256], c_t[:, :], wmod_sb[:, 512:768], start=True, stop=True).then_inc(s_mod[6], 1)
            eng.wait_ge(s_wa, 80)
            to_h_t(0)
            for gi in range(2):
                project(0, gi)
            project_v(0)
            for gi in range(2, 4):
                project(0, gi)
            eng.wait_ge(s_mod[7], 1)

            def unit(u, par, first, last):
                for s in range(4):
                    Q = u * 4 + s
                    bb, qd = s % 2, s // 2
                    if qd == 0:
                        for b in range(2):
                            eng.wait_ge(s_stk[b], (u * 2 + 1) * 16 * SECT)
                    else:
                        for b in range(2):
                            eng.wait_ge(s_stk[b], (u * 2 + 2) * 16 * SECT)
                    scores_half(Q, par, bb, qd, 0)
                    if s < 2 and not first:
                        to_y_token(u - 1, s)
                    if s >= 2 and not first:
                        to_h2_t(u - 1, s - 2, 2 * u)
                    if s == 2 and not last:
                        project_v(u + 1)
                    scores_half(Q, par, bb, qd, 1)
                    scores_2(Q, par, bb, qd)
                    if s == 0 and not first:
                        weighted(Q - 1, 1 - par, 1, 1, 1)
                    if s < 2 and not first:
                        to_y_d(u - 1, s)
                    if s >= 2 and not first:
                        route(u - 1, s - 2)
                    if s == 0 and not last:
                        to_h_t(u + 1)
                    if s > 0 and not last:
                        project(u + 1, s)
                    if s > 0:
                        weighted(Q - 1, par, (s - 1) % 2, (s - 1) % 2, (s - 1) // 2)
                    if s < 2 and not first:
                        project_out(u - 1, s)
                    if s == 0 and not last:
                        project(u + 1, 0)

            units(eng, unit)
            v = UNITS - 1
            to_y_token(v, 0)
            weighted(4 * UNITS - 1, 1, 1, 1, 1)
            for bb in range(2):
                if bb:
                    to_y_token(v, bb)
                to_y_d(v, bb)
                project_out(v, bb)
            for bb in range(2):
                to_h2_t(v, bb, 2 * v + 2)
                route(v, bb)
            eng.wait_ge(s_pr, 1)
            prf = pr[:, :, :].rearrange("p e t -> p (e t)")
            for h in range(2):
                k = tr(ps[:, 0, h * P:(h + 1) * P], prf[:, h * P:(h + 1) * P], ident[:, :])
            k.then_inc(s_ptp, 1)
            eng.wait_ge(s_cb, 2)
            eng.wait_ge(s_blk, 1)
            with eng.Fori(0, len(EXP_STEPS) + 1) as i:
                eng.wait_ge(s_cmp, i + 1)
                mm(ps[:, 1, 0:2], blk[:, :], cnt[:, 0:2], start=True, stop=True).then_inc(s_cnt, 1)
            with eng.Fori(0, QUARTERINGS) as i:
                eng.wait_ge(s_cmp, i + len(EXP_STEPS) + 2)
                mm(ps[:, 1, 0:6], blk[:, :], cnt[:, :], start=True, stop=True).then_inc(s_cnt, 1)
            eng.wait_ge(s_td, 1)
            mm(ps[:, 1, 8:8 + NE], ones_f[:, :], thr_d[:, :, :].rearrange("p h q -> p (h q)"), start=True, stop=True)\
                .then_inc(s_thp, 1)
            eng.wait_ge(s_seen, 1)
            flat = lambda a: a[:, :, :, :].rearrange("p a e t -> p (a e t)")
            mm(ps[:, 2, :], upper[:, :], flat(pick), start=True, stop=False)
            mm(ps[:, 2, :], ones_b[:, :], flat(seen_x), start=False, stop=True)
            mm(ps[:, 3, 0:NE], ones_b[:, :], seen[:, 0, :, NT - 1], start=True, stop=True).then_inc(s_posp, 1)
            for g in range(2):
                eng.wait_ge(s_oh, 4 * g + 4)
                for t in range(NT):
                    k = mm(ps[:, 4 + g, 0:P], oh_lo[:, 4 * g:4 * g + 4, :, t].rearrange("p e v -> p (e v)"),
                           oh_hi[:, 4 * g:4 * g + 4, :, :, t].rearrange("p e a v -> p (e a v)"),
                           start=(t == 0), stop=(t == NT - 1))
                k.then_inc(s_ixp, 1)
            eng.wait_ge(s_wf, 16 * (1 + NE))

            def to_x_t(e):
                eng.wait_ge(s_xg[e % 4], 16 * CT * (e // 4 + 1))
                if e >= 2:
                    eng.wait_ge(s_xt, e - 1)
                for j in range(CT):
                    k = tr(ps[:, 6 + e % 2, j * P:(j + 1) * P], xg[e % 4][:, j, 0:D], ident[:, :])
                k.then_inc(s_xtp, 1)

            to_x_t(0)
            for e in range(NE):
                eng.wait_ge(s_xt, e + 1)
                for k in range(FC):
                    if e:
                        eng.wait_ge(s_g, FC * (e - 1) + k + 1)
                    mm(ps[:, k, :], w1_sb[:, e, k * P:(k + 1) * P], x_t[e % 2], start=True, stop=True).then_inc(s_h1, 1)
                if e + 1 < NE:
                    to_x_t(e + 1)
                eng.wait_ge(s_g, FC * e + FC)
                if e >= 2:
                    eng.wait_ge(s_ob, e - 1)
                for j in range(CT):
                    for k in range(FC):
                        last = mm(ps[:, 4 + e % 2, j * P:(j + 1) * P], g_sb[:, k, j * P:(j + 1) * P], w2_sb[:, e, k, :],
                                  start=(k == 0), stop=(k == FC - 1))
                last.then_inc(s_op, 1)


def kernel(L0_attn_hidden_states, L0_attn_Wq, L0_attn_Wk, L0_attn_Wv, L0_attn_Wo, L0_ffn_Ws, L0_ffn_bs, L0_ffn_W1,
           L0_ffn_b1, L0_ffn_W2, L0_ffn_b2, L0_c, L0_wmod):
    import numpy as np
    import concourse.bacc as bacc
    from concourse import mybir as _mybir
    from concourse.bass_utils import run_bass_kernel_spmd

    a = np.asarray
    nb, seq, d = L0_attn_hidden_states.shape
    heads, fd, hd, p = 16, 16, 8, 128
    feat = lambda w: a(w).reshape(2, heads // 2, fd, d).transpose(3, 0, 2, 1).reshape(d, 2, 1, p)
    wqk = np.concatenate([feat(L0_attn_Wq), feat(L0_attn_Wk)], axis=2).reshape(d, 4 * p)
    wv = a(L0_attn_Wv).reshape(heads // 2, 2, hd, d).transpose(3, 1, 0, 2).reshape(d, d)
    ne, _, f = L0_ffn_W1.shape
    b1 = a(L0_ffn_b1).reshape(ne, f // p, p).transpose(2, 0, 1).reshape(p, ne * (f // p))
    ins = {
        "x": a(L0_attn_hidden_states).reshape(nb * seq, d), "wqk": wqk, "wv": wv, "wo": a(L0_attn_Wo).T,
        "ws": a(L0_ffn_Ws), "bs": a(L0_ffn_bs), "w1": a(L0_ffn_W1), "b1": b1, "w2": a(L0_ffn_W2), "b2": a(L0_ffn_b2),
        "c": a(L0_c), "wmod": a(L0_wmod),
    }
    nc = bacc.Bacc("TRN2", target_bir_lowering=False, num_devices=1)
    arrays, args = {}, []
    for name, v in ins.items():
        v = np.ascontiguousarray(v)
        arrays[f"in_{name}"] = v
        args.append(nc.dram_tensor(f"in_{name}", v.shape, _mybir.dt.from_np(v.dtype), kind="ExternalInput").ap())
    args.append(nc.dram_tensor("out_y", (nb * seq, d), _mybir.dt.float32, kind="ExternalOutput").ap())
    adaln_block_kernel(nc, *args)
    r = run_bass_kernel_spmd(nc, [arrays], core_ids=[0])
    return r.results[0]["out_y"].reshape(nb, seq, d)
```
